# Optimizing a Trainium2 kernel written in Bass

```python
import numpy as np
import jax
import jax.numpy as jnp

def _softmax(x, axis=-1):
    return jax.nn.softmax(x, axis=axis)

def _gelu(x):
    return jax.nn.gelu(x, approximate=True)

def _silu(x):
    return jax.nn.silu(x)

def _sigmoid(x):
    return jax.nn.sigmoid(x)

def _layernorm(x, axis=-1, eps=1e-05):
    m = jnp.mean(x, axis=axis, keepdims=True)
    v = jnp.var(x, axis=axis, keepdims=True)
    return (x - m) / jnp.sqrt(v + eps)

def _scatter_add(tgt, idx, src, axis=0):
    return tgt.at[idx].add(src)

def _segment_sum(src, seg, n):
    return jax.ops.segment_sum(src, seg, n)
kernel_name = 'mk_gnn_ffn_d1_gnn_r8_6e35b1'

def setup_inputs(seed: int=0):
    np.random.seed(seed)
    _w = jnp.asarray

    def _rec_inputs():
        import jax
        import jax.numpy as jnp
        _gk = jax.random.key(seed)
        x = -0.0003019 + 1 * jax.random.normal(jax.random.fold_in(_gk, 1), (1250, 1024), jnp.float32)
        src = jax.random.randint(jax.random.fold_in(_gk, 2), (20000,), 0, 1250, jnp.int32)
        dst = jnp.minimum((1250 * jax.random.uniform(jax.random.fold_in(_gk, 3), (20000,)) ** 2.0).astype(jnp.int32), 9999)
        _o = jnp.argsort(dst, stable=True)
        src = src[_o]
        dst = dst[_o]
        return (x, src, dst)
    x, src, dst = _rec_inputs()

    def _L0_gnn_setup():
        import jax, jax.numpy as jnp
        import numpy as np
        N = 2500
        E = 40000
        D_IN = 1024
        D_OUT = 1024
        key = jax.random.key(seed)
        k1, k2, k3, k4 = jax.random.split(key, 4)
        x = jax.random.normal(k1, (N, D_IN), dtype=jnp.float32)
        edge_index = jax.random.randint(k2, (2, E), 0, N, dtype=jnp.int64)
        W = jax.random.normal(k3, (D_OUT, D_IN), dtype=jnp.float32) * (1.0 / np.sqrt(D_IN))
        b = jax.random.normal(k4, (D_OUT,), dtype=jnp.float32) * 0.01
        return {'x': x, 'edge_index': edge_index, 'W': W, 'b': b}
    _L0_gnn_all = _L0_gnn_setup()
    _L0_gnn_in = {k: v for k, v in _L0_gnn_all.items() if k in ('W', 'b')}
    del _L0_gnn_all

    def _L0_ffn_setup():
        import jax, jax.numpy as jnp
        import numpy as np
        EPS = 1e-05

        def _quantize(W):
            gamma = jnp.mean(jnp.abs(W))
            return jnp.clip(jnp.round(W / (gamma + EPS)), -1.0, 1.0)
        key = jax.random.key(seed)
        k_x, k_w1, k_b1, k_w2, k_b2 = jax.random.split(key, 5)
        n_embd = 1024
        d_ff = 4 * n_embd
        B, S = (4, 512)
        bound1 = 1.0 / np.sqrt(n_embd)
        bound2 = 1.0 / np.sqrt(d_ff)
        x = jax.random.normal(k_x, (B, S, n_embd), dtype=jnp.float32)
        W1 = jax.random.uniform(k_w1, (d_ff, n_embd), jnp.float32, -bound1, bound1)
        b1 = jax.random.uniform(k_b1, (d_ff,), jnp.float32, -bound1, bound1)
        W2 = jax.random.uniform(k_w2, (n_embd, d_ff), jnp.float32, -bound2, bound2)
        b2 = jax.random.uniform(k_b2, (n_embd,), jnp.float32, -bound2, bound2)
        return {'x': x, 'W1': W1, 'b1': b1, 'W2': W2, 'b2': b2}
    _L0_ffn_all = _L0_ffn_setup()
    _L0_ffn_in = {k: v for k, v in _L0_ffn_all.items() if k in ('W1', 'b1', 'W2', 'b2')}
    del _L0_ffn_all
    return {'x': x, 'src': src, 'dst': dst, 'L0_gnn_W': _L0_gnn_in['W'], 'L0_gnn_b': _L0_gnn_in['b'], 'L0_ffn_W1': _L0_ffn_in['W1'], 'L0_ffn_b1': _L0_ffn_in['b1'], 'L0_ffn_W2': _L0_ffn_in['W2'], 'L0_ffn_b2': _L0_ffn_in['b2']}

def reference(x, src, dst, L0_gnn_W, L0_gnn_b, L0_ffn_W1, L0_ffn_b1, L0_ffn_W2, L0_ffn_b2):
    import jax
    import jax.numpy as jnp

    def _L0_gnn_ref(x, edge_index, W, b):
        import jax, jax.numpy as jnp
        import numpy as np
        N = 2500
        E = 40000
        D_IN = 1024
        D_OUT = 1024
        num_nodes = x.shape[0]
        self_idx = jnp.arange(num_nodes, dtype=edge_index.dtype)
        ei = jnp.concatenate([edge_index, jnp.stack([self_idx, self_idx], axis=0)], axis=1)
        row, col = (ei[0], ei[1])
        h = jnp.einsum('nd,od->no', x, W) + b
        deg = jnp.zeros((num_nodes,), dtype=h.dtype).at[row].add(1.0)
        deg_inv_sqrt = deg ** (-0.5)
        norm = deg_inv_sqrt[row] * deg_inv_sqrt[col]
        msg = norm[:, None] * h[col]
        out = jax.ops.segment_sum(msg, row, num_segments=num_nodes)
        return out

    def _L0_ffn_ref(x, W1, b1, W2, b2):
        import jax, jax.numpy as jnp
        import numpy as np
        EPS = 1e-05

        def _quantize(W):
            gamma = jnp.mean(jnp.abs(W))
            return jnp.clip(jnp.round(W / (gamma + EPS)), -1.0, 1.0)
        Wq1 = _quantize(W1)
        Wq2 = _quantize(W2)
        h = jax.nn.relu(jnp.einsum('bsd,fd->bsf', x, Wq1) + b1)
        out = jnp.einsum('bsf,df->bsd', h, Wq2) + b2
        return out
    edge_index = jnp.stack([src, dst])
    x = x + _L0_gnn_ref(_layernorm(x, axis=-1), edge_index, L0_gnn_W, L0_gnn_b)
    x = x + _L0_ffn_ref(_layernorm(x, axis=-1)[None], L0_ffn_W1, L0_ffn_b1, L0_ffn_W2, L0_ffn_b2)[0]
    return x

_drawn_inputs = setup_inputs


def setup_inputs(seed=0):
    import zlib

    import numpy as np

    out = dict(_drawn_inputs(seed))
    spreads = {}
    factors = {'L0_gnn_b': 7.337, 'L0_ffn_b1': 64.0, 'L0_ffn_b2': 64.0}
    for name, (base, spread) in spreads.items():
        noise = np.random.default_rng([zlib.crc32(name.encode()), seed]).standard_normal(out[name].shape)
        drawn = base * np.exp(spread * noise) if base else spread * noise
        out[name] = jnp.asarray(drawn.astype(out[name].dtype))
    for name, factor in factors.items():
        out[name] = (out[name] * factor).astype(out[name].dtype)
    return out
```

```python
from contextlib import ExitStack

import concourse.bass as bass
from concourse import mybir

F32 = mybir.dt.float32
F16 = mybir.dt.float16
BF16 = mybir.dt.bfloat16
F8 = mybir.dt.float8e4
I32 = mybir.dt.int32
ALU = mybir.AluOpType
ACT = mybir.ActivationFunctionType
AX = mybir.AxisListType

P = 128
NODES = 1250
EDGES = 20000
D = 1024
F = 4096
TILE = 125
NT = NODES // TILE
ET = EDGES // TILE
GROUP = 2
EG = ET // GROUP
KD = D // P
KF = F // P
HALF = D // 2
EPS = 1e-5
LNS = float(2 ** 10)
TOP = float(2 ** 14)
EXACT16 = 2048
EXPONENT = 0x7F800000
ROUND = 12582912.0
SRC_COLS = ((0, 417), (417, 417), (834, 416))
BLOCKS = ((0, 500), (500, 500), (1000, 250))
WCH = D
NCH = D * F // (P * WCH)
WG_LOADS = 4
WG_K = KD // WG_LOADS
RAW = 3
DEG_TILES = 16
DEG_CHUNKS = ET // DEG_TILES
DEG_RING = 6

A_WG = 2 * KD * NODES
A_SIZE = A_WG + 2 * KD * D
B_H = 0
B_C = 2 * NT * D
B_CLO = B_C + NT * NODES
B_OS = B_CLO + NT * NODES // 2
B_OD = B_OS + 2 * GROUP * NODES
B_IOTA = B_OD + 2 * GROUP * TILE
B_IDX = B_IOTA + NODES
B_W2 = 0
B_HID = KF * D // 2
B_SIZE = B_HID + KF * 2 * BLOCKS[0][1]
B_REST = B_IDX + 4 * ET
TURN_BANK, H_BANK, C_BANK, SUM_BANK = 0, 2, 4, 7
AGG_BANKS = (2, 4)
UP_BANKS = (6, 7, 2, 3)
DOWN_BANKS = (4, 0)


def gnn_ffn(nc, x, src_t, dst_t, dst_g, wg_t, bg, w1_t, b1, w2_t, b2, out):
    ctx = ExitStack()
    with ctx:
        def sb(name, shape, dt):
            return ctx.enter_context(nc.sbuf_tensor(name, shape, dt))

        def sem(name):
            return ctx.enter_context(nc.semaphore(name))

        area_a = sb("area_a", [P, A_SIZE], F16)
        area_b = sb("area_b", [P, B_SIZE], F16)
        xt = sb("xt", [P, 2, D], F32)
        xn = sb("xn", [P, 2, D], F32)
        ev = sb("ev", [P, 2, D], F32)
        raw = sb("raw", [P, RAW, WCH], F32)
        brow = sb("brow", [P, D], F32)
        ident = sb("ident", [P, P], F32)
        ones = sb("ones", [P, P], F32)
        pcol = sb("pcol", [P, 1], F32)
        b1s = sb("b1s", [P, KF], F32)
        small = sb("small", [P, 96], F32)
        small_i = sb("small_i", [P, 40], I32)
        ps = ctx.enter_context(nc.psum_tensor("ps", [P, 8, 512], F32))
        x1b = nc.dram_tensor("x1b", (NODES, D), F32).ap()

        ln_t = area_a[:, 0:A_WG].rearrange("p (s k n) -> p s k n", s=2, k=KD)
        wg = area_a[:, A_WG:A_SIZE].rearrange("p (s k n) -> p s k n", s=2, k=KD)
        wg_junk = area_a[:, A_WG:A_SIZE].bitcast(BF16)
        w1q = area_a[:, A_WG:A_SIZE].bitcast(F8).rearrange("p (k f) -> p k f", k=KD)
        wg_raw = area_b[:, 0:2 * KD * D].bitcast(F32).rearrange("p (k n) -> p k n", k=KD)
        h = area_b[:, B_H:B_C].rearrange("p (s j n) -> p s j n", s=2, j=NT)
        ct = area_b[:, B_C:B_CLO].rearrange("p (j n) -> p j n", j=NT)
        ct_lo = area_b[:, B_CLO:B_OS].bitcast(F8).rearrange("p (j n) -> p j n", j=NT)
        one_src = area_b[:, B_OS:B_OD].rearrange("p (s n) -> p s n", n=NODES)
        one_dst = area_b[:, B_OD:B_IOTA].rearrange("p (s n) -> p s n", n=TILE)
        iota = area_b[:, B_IOTA:B_IDX]
        idx = area_b[:, B_IDX:B_IDX + 4 * ET].bitcast(F32)
        src_f, dst_f = idx[:, 0:ET], idx[:, ET:2 * ET]
        hot_size = DEG_TILES * TILE
        hot_lo = area_b[:, B_C:B_C + DEG_RING * hot_size].rearrange("p (r n c) -> p r n c", r=DEG_RING, c=DEG_TILES)
        b_rep = B_C + DEG_RING * hot_size
        iota_rep = area_b[:, b_rep:b_rep + hot_size].rearrange("p (n c) -> p n c", c=DEG_TILES)
        hot_hi = area_b[:, b_rep + hot_size:b_rep + hot_size + ET * NT].rearrange("p (c n) -> p c n", c=ET)
        src_lo = area_b[:, b_rep + hot_size + ET * NT:b_rep + hot_size + ET * NT + ET]
        ident16 = area_b[:, B_REST:B_REST + P]
        wabs = area_b[:, B_REST + P:B_REST + P + 4 * NCH].bitcast(F32).rearrange(
            "p (w m) -> p w m", w=2)
        run = area_b[:, B_REST + P + 4 * NCH:B_REST + P + 4 * NCH + 4 * NT].bitcast(F32).rearrange(
            "p (s t) -> p s t", s=2)
        tile_start = area_b[:, B_REST + P + 4 * NCH + 4 * NT:B_REST + P + 4 * NCH + 6 * NT].bitcast(F32)
        idx_i = ev[:, 0, 0:2 * ET].bitcast(I32)
        idx_g = ev[:, 0, 2 * ET:2 * ET + EDGES // EG].bitcast(I32)
        src_hi = ev[:, 1, 0:ET]
        w2q = area_b[:, B_W2:B_HID].bitcast(F8).rearrange("p (f n) -> p f n", f=KF)
        hid = area_b[:, B_HID:B_SIZE].rearrange("p (f s n) -> p f s n", f=KF, s=2)

        def col(a, n=1):
            return small[:, a:a + n]
        edge_max, edge_min = col(0), col(1)
        rel_a, rel_b = col(2, NT), col(12, NT)
        votes, voted = col(22, 2 * NT), col(42, 2 * NT)
        deg, dinv = col(62, NT), col(72, NT)
        h_scale, out_scale = rel_a, rel_b
        peak, peak_all = col(82), col(83)
        deg_max = col(1)
        sumsq, root, bound, back = col(84, 3), col(87, 3), col(90, 3), col(93, 3)
        stats = sb("stats", [P, 2, 12], F32)
        mean_var = sb("mean_var", [P, 2, 2], F32)
        std = sb("std", [P, 2], F32)
        rstd = sb("rstd", [P, 2], F32)
        eps = sb("eps", [P, 1], F32)
        part = sb("part", [P, 4], F32)
        wg_sq = sb("wg_sq", [P, WG_LOADS], F32)
        scal = sb("scal", [P, 16], F32)
        s_w = scal[:, 0:1]
        s_hq = scal[:, 1:2]
        s_hid = scal[:, 2:3]
        i_w, i_hq, i_hid = scal[:, 3:4], scal[:, 4:5], scal[:, 5:6]
        s_psum_h = scal[:, 6:7]
        s_psum_hid = scal[:, 7:8]
        thr = scal[:, 8:10]

        edges_in, bg_in, b1_in, b2_in = sem("edges_in"), sem("bg_in"), sem("b1_in"), sem("b2_in")
        wg_in = [sem(f"wg_in{s}") for s in range(WG_LOADS)]
        x_in = [sem("x_in0"), sem("x_in1")]
        raw_in = [sem(f"raw_in{r}") for r in range(RAW)]
        iota_done, pcol_done, votes_in, votes_done = sem("iota_done"), sem("pcol_done"), sem("votes_in"), sem("votes_done")
        consts_done, table_done = sem("consts_done"), sem("table_done")
        squares_done, squares_in, squares_sum = sem("squares_done"), sem("squares_in"), sem("squares_sum")
        sumsq_done, root_done, scales_done = sem("sumsq_done"), sem("root_done"), sem("scales_done")
        wg_hi_done, wg_done = sem("wg_hi_done"), sem("wg_done")
        hot_done, hot_used = sem("hot_done"), sem("hot_used")
        deg_done, deg_root, peak_in, peak_done, degrees_done = (
            sem("deg_done"), sem("deg_root"), sem("peak_in"), sem("peak_done"), sem("degrees_done"))
        var_done, std_done, xn_done = sem("var_done"), sem("std_done"), sem("xn_done")
        turned, turned_hi, ln_done = sem("turned"), sem("turned_hi"), sem("ln_done")
        hot = [sem("hot0"), sem("hot1")]
        hot_free = [sem("hot_free0"), sem("hot_free1")]
       
        c_done, c_hi, c_out = sem("c_done"), sem("c_hi"), sem("c_out")
        h_done, h_out, h_hi, h_ready = sem("h_done"), sem("h_out"), sem("h_hi"), sem("h_ready")
        h_scaled, turned_f32, wg_scaled = sem("h_scaled"), sem("turned_f32"), sem("wg_scaled")
        agg_done, x1_done, x1b_done = sem("agg_done"), sem("x1_done"), sem("x1b_done")
        x1b_stored = [sem("x1b_stored0"), sem("x1b_stored1")]
        w_summed, w_sum_in, w_sum, thr_done = sem("w_summed"), sem("w_sum_in"), sem("w_sum"), sem("thr_done")
        w_sign, w_quant = sem("w_sign"), sem("w_quant")
        up_done, hid_hi = sem("up_done"), sem("hid_hi")
        up_free, relu_free = sem("up_free"), sem("relu_free")
        down_done, res_in, out_done = (
            sem("down_done"), [sem("res_in0"), sem("res_in1")], sem("out_done"))
        stored = [sem("stored0"), sem("stored1")]
        dve_step = sem("dve_step")

        def load_table(eng, t):
            return (eng.value_load(small_i[0:1, 3 * t:3 * t + 1], min_val=0, max_val=EG - 2),
                    eng.value_load(small_i[0:1, 3 * t + 1:3 * t + 2], min_val=1, max_val=EG // 2),
                    eng.value_load(small_i[0:1, 3 * t + 2:3 * t + 3], min_val=0, max_val=NT * EG // 2))

        def load_peak(eng):
            return eng.value_load(small_i[0:1, 3 * NT:3 * NT + 1], min_val=0, max_val=EDGES + 1)

        def edge_tile(first, step, half):
            return nc.s_assert_within((first + step * 2 + half) * GROUP, 0, ET - GROUP,
                                      skip_runtime_bounds_check_because="first + 2 steps <= EG by the table")

        def relu_tile(u, number):
            return xn[:, u // 2, (u % 2) * HALF:(u % 2) * HALF + number].unsqueeze(1)

        def chunk_src(n):
            w, m = (n // NCH) % 2, n % NCH
            if w:
                return w2_t[m * P:(m + 1) * P, :]
            k, q = m // (F // WCH), m % (F // WCH)
            return w1_t[k * P:(k + 1) * P, q * WCH:(q + 1) * WCH]

        def quantised(n):
            w, m = (n // NCH) % 2, n % NCH
            if w:
                return w2q[:, m, :]
            k, q = m // (F // WCH), m % (F // WCH)
            return w1q[:, k, q * WCH:(q + 1) * WCH]

        SUM_AT = [7] * 9 + [2 * NCH - 63]
        QUANT_AT = [3] * 8 + [4, 4]

        block = ctx.enter_context(nc.Block())

        def store_out(sp, i):
            sp.wait_ge(out_done, i + 3)
            sp.dma_start(out[i * TILE:(i + 1) * TILE, :], ev[0:TILE, i % 2, :]).then_inc(stored[i % 2], 16)

        @block.sync
        def _(sp):
            sent = [0]

            def load_chunk():
                n = sent[0]
                if n >= RAW:
                    free = n - RAW + 1
                    if free <= 2 * NCH:
                        sp.wait_ge(w_summed, free)
                    else:
                        sp.wait_ge(w_quant, free - 2 * NCH)
                sp.dma_start(raw[:, n % RAW, :], chunk_src(n)).then_inc(raw_in[n % RAW], 16)
                sent[0] += 1

            def load_x(k):
                t = k % NT
                if 2 <= k < NT + 2:
                    sp.wait_ge(xn_done, k - 1)
                elif k >= NT + 2:
                    sp.wait_ge(x1_done, k - NT - 1)
                sp.dma_start(xt[0:TILE, k % 2, :], x[t * TILE:(t + 1) * TILE, :]).then_inc(x_in[k % 2], 16)

            sp.dma_start(idx_i[0:TILE, 0:ET], src_t).then_inc(edges_in, 16)
            sp.dma_start(idx_i[0:TILE, ET:2 * ET], dst_t).then_inc(edges_in, 16)
            sp.dma_start(idx_g[0:EG, :], dst_g).then_inc(edges_in, 16)
            load_x(0)
            for s in range(WG_LOADS):
                sp.dma_start(wg_raw[:, s * WG_K:(s + 1) * WG_K, :],
                             wg_t[s * WG_K * P:(s + 1) * WG_K * P, :].rearrange("(k p) n -> p k n", p=P)
                             ).then_inc(wg_in[s], 16)
            sp.dma_start(brow[:, :], bg.partition_broadcast(P)).then_inc(bg_in, 16)
            sp.dma_start(b1s[:, :], b1).then_inc(b1_in, 16)
            load_x(1)
            for t in range(NT):
                if t + 2 < NT:
                    load_x(t + 2)
                for _ in range(SUM_AT[t]):
                    load_chunk()
            sp.wait_ge(h_out, NT)
            sp.dma_start(brow[:, :], b2.partition_broadcast(P)).then_inc(b2_in, 16)
            load_x(NT)
            load_x(NT + 1)
            for i in range(NT):
                for _ in range(QUANT_AT[i]):
                    load_chunk()
                if i + 2 < NT:
                    load_x(NT + i + 2)
            for _ in range(NCH):
                load_chunk()
            for s in range(2):
                sp.wait_ge(x1b_stored[s], 16 * NT // 2)
            for i in range(NT):
                if i < 2:
                    sp.wait_ge(x1_done, NT)
                else:
                    sp.wait_ge(out_done, i + 1)
                sp.dma_start(xt[0:TILE, i % 2, :], x1b[i * TILE:(i + 1) * TILE, :]).then_inc(res_in[i % 2], 16)
                if i >= 2:
                    store_out(sp, i - 2)
            for i in (NT - 2, NT - 1):
                store_out(sp, i)
            for s in range(2):
                sp.wait_ge(stored[s], 16 * NT // 2)

        @block.gpsimd
        def _(pool):
            nc.gpsimd.iota(iota[:, :], pattern=[[1, NODES]], base=0, channel_multiplier=0,
                           allow_small_or_imprecise_dtypes=True).then_inc(iota_done, 1)
            nc.gpsimd.iota(pcol[:, :], pattern=[[1, 1]], base=0, channel_multiplier=1,
                           allow_small_or_imprecise_dtypes=True).then_inc(pcol_done, 1)
            nc.gpsimd.iota(tile_start[:, :], pattern=[[TILE, NT]], base=0, channel_multiplier=0,
                           allow_small_or_imprecise_dtypes=True).then_inc(pcol_done, 1)
            nc.gpsimd.iota(iota_rep[:, :, :], pattern=[[1, TILE], [0, DEG_TILES]], base=0, channel_multiplier=0,
                           allow_small_or_imprecise_dtypes=True).then_inc(pcol_done, 1)
            pool.wait_ge(votes_in, 1)
            nc.gpsimd.partition_all_reduce(voted, votes, P, bass.bass_isa.ReduceOp.max).then_inc(votes_done, 1)
            pool.wait_ge(peak_in, 1)
            nc.gpsimd.partition_all_reduce(peak_all, peak, P, bass.bass_isa.ReduceOp.max).then_inc(peak_done, 1)

            for k in range(KD):
                pool.wait_ge(wg_hi_done, k + 1)
                nc.gpsimd.tensor_tensor(wg[:, 1, k, :], wg_raw[:, k, :], wg[:, 0, k, :],
                                        ALU.subtract).then_inc(wg_done, 1)

            def ln_low(k):
                t = k % NT
                pool.wait_ge(turned_hi, k + 1)
                nc.gpsimd.tensor_tensor(
                    ln_t[:, 1, :, t * TILE:(t + 1) * TILE],
                    xn[:, k % 2, 0:KD * TILE].rearrange("p (b n) -> p b n", b=KD),
                    ln_t[:, 0, :, t * TILE:(t + 1) * TILE], ALU.subtract).then_inc(ln_done, 1)

            def h_low(t):
                pool.wait_ge(h_hi, t + 1)
                nc.gpsimd.tensor_tensor(h[0:TILE, 1, t, :], ev[0:TILE, t % 2, :], h[0:TILE, 0, t, :],
                                        ALU.subtract).then_inc(h_ready, 1)

            ln_low(0)
            for t in range(NT):
                if t >= 1:
                    h_low(t - 1)
                if t + 1 < NT:
                    ln_low(t + 1)
            h_low(NT - 1)

            pool.wait_ge(b2_in, 16)
            for i in range(NT):
                pool.wait_ge(xn_done, NT + i + 1)
                nc.gpsimd.tensor_tensor(ev[0:TILE, i % 2, :], ev[0:TILE, i % 2, :], brow[0:TILE, :],
                                        ALU.add).then_inc(x1b_done, 1)
                pool.wait_ge(x1b_done, i + 1)
                pool.dma_start(x1b[i * TILE:(i + 1) * TILE, :], ev[0:TILE, i % 2, :]).then_inc(x1b_stored[i % 2], 16)
                if i >= 1:
                    ln_low(NT + i - 1)
            ln_low(2 * NT - 1)

        @block.scalar
        def _(act):
            def ln_std(k):
                act.wait_ge(var_done, k + 1)
                nc.scalar.activation(std[0:TILE, k % 2:k % 2 + 1], mean_var[0:TILE, k % 2, 1:2], ACT.Sqrt,
                                     scale=LNS ** -2, bias=eps[0:TILE, :]).then_inc(std_done, 1)

            def ln_hi(k):
                t = k % NT
                act.wait_ge(turned, k + 1)
                turned_ps = ps[:, TURN_BANK:TURN_BANK + 2, 0:4 * TILE]
                nc.scalar.activation(xn[:, k % 2, 0:KD * TILE].rearrange("p (a n) -> p a n", a=2), turned_ps, ACT.Copy)
                if k == NT:
                    act.wait_ge(h_done, NT)
                nc.scalar.activation(ln_t[:, 0, :, t * TILE:(t + 1) * TILE].rearrange("p (a b) n -> p a b n", a=2),
                                     turned_ps.rearrange("p a (b n) -> p a b n", b=4),
                                     ACT.Copy).then_inc(turned_hi, 1)

            ln_std(0)
            for s in range(WG_LOADS):
                act.wait_ge(wg_in[s], 16)
                nc.scalar.activation(wg_junk[:, s * WG_K * D:(s + 1) * WG_K * D],
                                     wg_raw[:, s * WG_K:(s + 1) * WG_K, :].rearrange("p k n -> p (k n)"),
                                     ACT.Square, accum_out=wg_sq[:, s:s + 1]).then_inc(squares_done, 1)
            act.wait_ge(b1_in, 16)
            nc.scalar.activation(wg_junk[:, KD * D:KD * D + KF], b1s[:, :], ACT.Square,
                                 accum_out=part[:, 2:3]).then_inc(squares_done, 1)
            act.wait_ge(bg_in, 16)
            nc.scalar.activation(wg_junk[:, KD * D + KF:KD * D + KF + D], brow[:, :], ACT.Square,
                                 accum_out=part[:, 3:4]).then_inc(squares_done, 1)
            ln_std(1)
            act.wait_ge(deg_done, 1)
            nc.scalar.activation(dinv[0:TILE, :], deg[0:TILE, :], ACT.Sqrt).then_inc(deg_root, 1)
            act.wait_ge(sumsq_done, 1)
            nc.scalar.activation(root, sumsq, ACT.Sqrt).then_inc(root_done, 1)
            act.wait_ge(scales_done, 1)
            for k in range(KD):
                nc.scalar.activation(wg[:, 0, k, :], wg_raw[:, k, :], ACT.Copy, scale=s_w).then_inc(wg_scaled, 1)
                act.wait_ge(wg_scaled, 2 * k + 1)
                nc.scalar.activation(wg_raw[:, k, :], wg_raw[:, k, :], ACT.Copy, scale=s_w).then_inc(wg_scaled, 1)
                act.wait_ge(wg_scaled, 2 * k + 2)
                act.sem_inc(wg_hi_done, 1)
            ln_hi(0)

            def sum_chunks(first, number):
                for n in range(first, first + number):
                    act.wait_ge(raw_in[n % RAW], 16 * (n // RAW + 1))
                    nc.scalar.activation(raw[:, n % RAW, :], raw[:, n % RAW, :], ACT.Abs,
                                         accum_out=wabs[:, n // NCH, n % NCH:n % NCH + 1]).then_inc(w_summed, 1)

            def h_high(t):
                act.wait_ge(h_out, t + 1)
                nc.scalar.activation(ev[0:TILE, t % 2, :], ev[0:TILE, t % 2, :], ACT.Copy,
                                     scale=h_scale[0:TILE, t:t + 1]).then_inc(h_scaled, 1)
                act.wait_ge(h_scaled, t + 1)
                nc.scalar.activation(h[0:TILE, 0, t, :], ev[0:TILE, t % 2, :], ACT.Copy).then_inc(h_hi, 1)

            n = 0
            for t in range(NT):
                if t >= 1:
                    h_high(t - 1)
                act.wait_ge(c_done, t + 1)
                if t == 0:
                    act.wait_ge(hot_used, DEG_CHUNKS)
                for b, (a, w) in enumerate(SRC_COLS):
                    last = nc.scalar.activation(ct[0:TILE, t, a:a + w], ps[0:TILE, C_BANK + b, 0:w], ACT.Copy)
                last.then_inc(c_hi, 1)
                if t + 1 < NT:
                    ln_hi(t + 1)
                if t + 2 < NT:
                    ln_std(t + 2)
                sum_chunks(n, SUM_AT[t])
                n += SUM_AT[t]
            h_high(NT - 1)
            def signs(m):
                n = 2 * NCH + m
                w = (n // NCH) % 2
                if m == 0:
                    act.wait_ge(thr_done, 1)
                    act.wait_ge(h_done, NT)
                if m == NCH:
                    act.wait_ge(agg_done, NT)
                act.wait_ge(raw_in[n % RAW], 16 * (n // RAW + 1))
                nc.scalar.activation(quantised(n), raw[:, n % RAW, :], ACT.Sign,
                                     bias=thr[:, w:w + 1], saturate=False).then_inc(w_sign, 1)

            m = 0
            for i in range(NT):
                ln_std(NT + i)
                for _ in range(QUANT_AT[i]):
                    signs(m)
                    m += 1
                if i >= 1:
                    ln_hi(NT + i - 1)
            ln_hi(2 * NT - 1)

            def hid_high(before, f, u, number):
                act.wait_ge(up_done, before + 1)
                act.wait_ge(relu_free, before + 1)
                r = relu_tile(u, number)
                nc.scalar.activation(r, ps[:, UP_BANKS[u], 0:number].unsqueeze(1), ACT.Relu,
                                     scale=s_psum_hid, bias=b1s[:, bass.ds(f, 1)]).then_inc(up_free, 1)
                act.wait_ge(up_free, before + 5)
                nc.scalar.activation(hid[:, bass.ds(f, 1), 0, 0:number], r, ACT.Copy).then_inc(hid_hi, 1)

            for b, (first, number) in enumerate(BLOCKS):
                if b:
                    act.wait_ge(down_done, first // TILE)
                if b == 0:
                    for f in range(KF):
                        if f == 0:
                            signs(NCH)
                        if f + 1 < KF:
                            signs(NCH + f + 1)
                        if f == 0 or f == 2:
                            act.wait_ge(ln_done, 2 * NT - 1 + f // 2)
                        hid_high(f, f, f % 4, number)
                else:
                    with act.Fori(0, KF // 4) as q:
                        for u in range(4):
                            hid_high(q * 4 + (b * KF + u), q * 4 + u, u, number)

        @block.vector
        def _(dve):
            steps = [0]

            def settle(ins):
                steps[0] += 1
                ins.then_inc(dve_step, 1)
                dve.wait_ge(dve_step, steps[0])

            nc.vector.memset(small[:, :], 0.0)
            nc.vector.memset(ones[:, :], 1.0)
            settle(nc.vector.memset(eps[:, :], EPS * LNS ** -2))
            dve.wait_ge(iota_done, 1)
            dve.wait_ge(pcol_done, 3)
            nc.vector.tensor_scalar(ident[:, :], iota[:, 0:P], pcol[:, :], None, ALU.is_equal)
            nc.vector.tensor_scalar(ident16[:, :], iota[:, 0:P], pcol[:, :], None,
                                    ALU.is_equal).then_inc(consts_done, 1)
            dve.wait_ge(edges_in, 48)
            nc.vector.tensor_copy(idx[0:TILE, :], idx_i[0:TILE, :])

            nc.vector.tensor_reduce(edge_max[0:EG, :], idx_g[0:EG, :], AX.X, ALU.max)
            settle(nc.vector.tensor_reduce(edge_min[0:EG, :], idx_g[0:EG, :], AX.X, ALU.min))
            nc.vector.tensor_scalar(rel_a[0:EG, :], tile_start[0:EG, :], edge_max[0:EG, :], None, ALU.is_le)
            settle(nc.vector.tensor_scalar(rel_b[0:EG, :], tile_start[0:EG, :], edge_min[0:EG, :], -float(TILE),
                                           ALU.subtract, ALU.is_gt))
            settle(nc.vector.tensor_tensor(rel_a[0:EG, :], rel_a[0:EG, :], rel_b[0:EG, :], ALU.mult))
            nc.vector.tensor_scalar(peak[0:EG, :], pcol[0:EG, :], -1.0, float(EG), ALU.mult, ALU.add)
            settle(nc.vector.tensor_scalar(peak_all[0:EG, :], pcol[0:EG, :], 1.0, None, ALU.add))
            nc.vector.tensor_scalar(votes[0:EG, 0:NT], rel_a[0:EG, :], peak_all[0:EG, :], None, ALU.mult)
            nc.vector.tensor_scalar(votes[0:EG, NT:2 * NT], rel_a[0:EG, :], peak[0:EG, :], None,
                                    ALU.mult).then_inc(votes_in, 1)

            def ln_stats(k):
                s = k % 2
                if k < NT:
                    dve.wait_ge(x_in[s], 16 * (k // 2 + 1))
                    rows = xt[0:TILE, s, :]
                else:
                    rows = ev[0:TILE, s, :]
                for b in range(2):
                    last = nc.vector.bn_stats(stats[0:TILE, s, 6 * b:6 * b + 6], rows[:, b * HALF:(b + 1) * HALF])
                settle(last)
                nc.vector.bn_aggr(mean_var[0:TILE, s, :], stats[0:TILE, s, :]).then_inc(var_done, 1)

            def ln_apply(k):
                s = k % 2
                dve.wait_ge(std_done, k + 1)
                settle(nc.vector.reciprocal(rstd[0:TILE, s:s + 1], std[0:TILE, s:s + 1]))
                if k >= 2:
                    dve.wait_ge(ln_done, k - 1)
                rows = xt[0:TILE, s, :] if k < NT else ev[0:TILE, s, :]
                nc.vector.tensor_scalar(xn[0:TILE, s, :], rows, mean_var[0:TILE, s, 0:1], rstd[0:TILE, s:s + 1],
                                        ALU.subtract, ALU.mult).then_inc(xn_done, 1)

            ln_stats(0)

            settle(nc.vector.tensor_scalar(src_hi[0:TILE, :], src_f[0:TILE, :], 1.0 / TILE, 0.5 / TILE - 0.5,
                                           ALU.mult, ALU.add))
            settle(nc.vector.tensor_scalar(src_hi[0:TILE, :], src_hi[0:TILE, :], ROUND, -ROUND, ALU.add, ALU.add))
            settle(nc.vector.scalar_tensor_tensor(src_lo[0:TILE, :], src_hi[0:TILE, :], -float(TILE),
                                                  src_f[0:TILE, :], ALU.mult, ALU.add))
            ln_apply(0)
            nc.vector.tensor_tensor(hot_hi[0:TILE, :, :],
                                    iota[0:TILE, 0:NT].unsqueeze(1).broadcast_to((TILE, ET, NT)),
                                    src_hi[0:TILE, :].unsqueeze(2).broadcast_to((TILE, ET, NT)), ALU.is_equal)
            def degree_chunk(c):
                if c >= DEG_RING:
                    dve.wait_ge(hot_used, c - DEG_RING + 1)
                nc.vector.tensor_tensor(
                    hot_lo[0:TILE, c % DEG_RING, :, :], iota_rep[0:TILE, :, :],
                    src_lo[0:TILE, c * DEG_TILES:(c + 1) * DEG_TILES].unsqueeze(1).broadcast_to((TILE, TILE, DEG_TILES)),
                    ALU.is_equal).then_inc(hot_done, 1)

            for c in range(DEG_CHUNKS // 2):
                degree_chunk(c)

            dve.wait_ge(votes_done, 1)
            last_group, first_group = voted[:, 0:NT], voted[:, NT:2 * NT]
            settle(nc.vector.tensor_scalar(first_group, first_group, -1.0, float(EG), ALU.mult, ALU.add))
            settle(nc.vector.tensor_tensor(last_group, last_group, first_group, ALU.subtract))
            settle(nc.vector.tensor_scalar(last_group, last_group, 0.5, 0.25, ALU.mult, ALU.add))
            settle(nc.vector.tensor_scalar(last_group, last_group, 1.0, ROUND, ALU.max, ALU.add))
            settle(nc.vector.tensor_scalar(last_group, last_group, -ROUND, None, ALU.add))
            settle(nc.vector.tensor_scalar(run[:, 1, :], last_group, -2.0, float(EG), ALU.mult, ALU.add))
            settle(nc.vector.tensor_tensor(first_group, first_group, run[:, 1, :], ALU.min))
            nc.vector.memset(run[:, 0, 0:1], 0.0)
            settle(nc.vector.tensor_copy(run[:, 0, 1:NT], last_group[:, 0:NT - 1]))
            a, shift = 0, 1
            while shift < NT:
                nc.vector.tensor_copy(run[:, 1 - a, 0:shift], run[:, a, 0:shift])
                settle(nc.vector.tensor_tensor(run[:, 1 - a, shift:NT], run[:, a, shift:NT],
                                               run[:, a, 0:NT - shift], ALU.add))
                a, shift = 1 - a, 2 * shift
            table = small_i[:, 0:3 * NT].rearrange("p (t c) -> p c t", c=3)
            nc.vector.tensor_copy(table[:, 0, :], first_group)
            nc.vector.tensor_copy(table[:, 1, :], last_group)
            nc.vector.tensor_copy(table[:, 2, :], run[:, a, :]).then_inc(table_done, 1)

            for c in range(DEG_CHUNKS // 2, DEG_CHUNKS):
                degree_chunk(c)
            ln_stats(1)
            ln_apply(1)
            dve.wait_ge(hot_used, DEG_CHUNKS)
            settle(nc.vector.tensor_scalar(deg[0:TILE, :], ps[0:TILE, SUM_BANK, 0:NT], 1.0, None, ALU.add))
            nc.vector.memset(peak, 0.0)
            settle(nc.vector.tensor_reduce(deg_max[0:TILE, :], deg[0:TILE, :], AX.X, ALU.max))
            nc.vector.tensor_copy(peak[0:TILE, :], deg_max[0:TILE, :]).then_inc(peak_in, 1)
            dve.wait_ge(peak_in, 1)
            dve.sem_inc(deg_done, 1)

            dve.wait_ge(squares_done, WG_LOADS + 2)
            nc.vector.tensor_copy(part[:, 1:2], part[:, 2:3])
            nc.vector.tensor_reduce(part[:, 0:1], wg_sq[:, :], AX.X, ALU.add).then_inc(squares_in, 1)
            dve.wait_ge(squares_sum, 1)
            nc.vector.tensor_copy(sumsq[:, 0:2], ps[:, H_BANK + 1, 0:2])
            nc.vector.tensor_copy(sumsq[:, 2:3], part[:, 3:4]).then_inc(sumsq_done, 1)
            dve.wait_ge(root_done, 1)
            settle(nc.vector.scalar_tensor_tensor(root[:, 2:3], root[:, 0:1], D ** 0.5, root[:, 2:3],
                                                  ALU.mult, ALU.add))
            nc.vector.tensor_scalar(bound[:, 0:1], root[:, 0:1], 1e-30, None, ALU.max)
            nc.vector.tensor_scalar(bound[:, 1:2], root[:, 2:3], 1e-30, None, ALU.max)
            settle(nc.vector.tensor_scalar(bound[:, 2:3], root[:, 1:2], float(D), None, ALU.add))
            settle(nc.vector.tensor_scalar(bound.bitcast(I32), bound.bitcast(I32), EXPONENT, None,
                                           ALU.bitwise_and))
            settle(nc.vector.reciprocal(back, bound))
            nc.vector.tensor_scalar(scal[:, 0:3], back, TOP, None, ALU.mult)
            nc.vector.tensor_scalar(scal[:, 3:6], bound, 1.0 / TOP, None, ALU.mult)
            nc.vector.tensor_scalar(s_psum_h, bound[:, 0:1], 1.0 / (TOP * LNS), None, ALU.mult)
            settle(nc.vector.tensor_scalar(s_psum_hid, back[:, 2:3], TOP / LNS, None, ALU.mult))
            nc.vector.tensor_scalar(b1s[:, :], b1s[:, :], s_hid, None, ALU.mult).then_inc(scales_done, 1)
            dve.wait_ge(deg_root, 1)
            settle(nc.vector.reciprocal(dinv[0:TILE, :], dinv[0:TILE, :]))
            nc.vector.tensor_scalar(h_scale[0:TILE, :], dinv[0:TILE, :], s_hq[0:TILE, :], None, ALU.mult)
            settle(nc.vector.tensor_scalar(out_scale[0:TILE, :], dinv[0:TILE, :], i_hq[0:TILE, :], None, ALU.mult))
            dve.wait_ge(peak_done, 1)
            nc.vector.tensor_copy(small_i[:, 3 * NT:3 * NT + 1], peak_all).then_inc(degrees_done, 1)
            dve.wait_ge(degrees_done, 1)
            dve.wait_ge(table_done, 1)
            largest = load_peak(dve)

            def h_leave(t):
                dve.wait_ge(h_done, t + 1)
                if t == 0:
                    dve.wait_ge(bg_in, 16)
                if t >= 2:
                    dve.wait_ge(h_ready, t - 1)
                for b in range(2):
                    last = nc.vector.scalar_tensor_tensor(
                        ev[0:TILE, t % 2, b * HALF:(b + 1) * HALF], ps[0:TILE, H_BANK + b, :], s_psum_h[0:TILE, :],
                        brow[0:TILE, b * HALF:(b + 1) * HALF], ALU.mult, ALU.add)
                last.then_inc(h_out, 1)

            for t in range(NT):
                first, number, before = load_table(dve, t)
                dve.wait_ge(hot_free[0], before + t + 1)
                nc.vector.tensor_scalar(one_src[0:TILE, 0, :], iota[0:TILE, :], pcol[0:TILE, :], float(t * TILE),
                                        ALU.subtract, ALU.is_equal).then_inc(hot[0], 1)
                with dve.Fori(0, number) as step:
                    for v in range(2):
                        c = edge_tile(first, step, v)
                        dve.wait_ge(hot_free[v], before + step + (1 if v else t + 2))
                        nc.vector.tensor_tensor(
                            one_dst[0:TILE, v * GROUP:(v + 1) * GROUP, :],
                            iota[0:TILE, t * TILE:(t + 1) * TILE].unsqueeze(1).broadcast_to((TILE, GROUP, TILE)),
                            dst_f[0:TILE, bass.ds(c, GROUP)].unsqueeze(2).broadcast_to((TILE, GROUP, TILE)),
                            ALU.is_equal)
                        for g in range(GROUP):
                            last = nc.vector.tensor_scalar(one_src[0:TILE, v * GROUP + g, :], iota[0:TILE, :],
                                                           src_f[0:TILE, bass.ds(c + g, 1)], None, ALU.is_equal)
                        last.then_inc(hot[v], 1)
                if t >= 1:
                    h_leave(t - 1)
                if t + 2 < NT:
                    ln_stats(t + 2)
                with dve.If(largest > EXACT16):
                    dve.wait_ge(c_hi, t + 1)
                    for b, (a, w) in enumerate(SRC_COLS):
                        nc.vector.tensor_tensor(ct_lo[0:TILE, t, a:a + w], ps[0:TILE, C_BANK + b, 0:w],
                                                ct[0:TILE, t, a:a + w], ALU.subtract, saturate=False)
                dve.drain().then_inc(c_out, 1)
                if t + 2 < NT:
                    ln_apply(t + 2)
            h_leave(NT - 1)

            dve.wait_ge(w_summed, 2 * NCH)
            nc.vector.tensor_reduce(part[:, 0:2], wabs[:, :, :], AX.X, ALU.add).then_inc(w_sum_in, 1)
            dve.wait_ge(w_sum, 1)
            settle(nc.vector.tensor_scalar(thr, ps[:, SUM_BANK, 0:2], 1.0 / (D * F), EPS, ALU.mult, ALU.add))
            nc.vector.tensor_scalar(thr, thr, 0.5, None, ALU.mult).then_inc(thr_done, 1)

            def quantise(m):
                n = 2 * NCH + m
                w = (n // NCH) % 2
                dve.wait_ge(w_sign, m + 1)
                nc.vector.scalar_tensor_tensor(quantised(n), raw[:, n % RAW, :], thr[:, w:w + 1], quantised(n),
                                               ALU.is_gt, ALU.min, saturate=False).then_inc(w_quant, 1)

            m = 0
            for i in range(NT):
                dve.wait_ge(agg_done, i + 1)
                dve.wait_ge(x_in[i % 2], 16 * ((NT + i) // 2 + 1))
                if i >= 2:
                    dve.wait_ge(x1b_stored[i % 2], 16 * (i // 2))
                else:
                    dve.wait_ge(h_ready, NT - 1 + i)
                for b in range(2):
                    last = nc.vector.scalar_tensor_tensor(
                        ev[0:TILE, i % 2, b * HALF:(b + 1) * HALF], ps[0:TILE, AGG_BANKS[i % 2] + b, :],
                        out_scale[0:TILE, i:i + 1], xt[0:TILE, i % 2, b * HALF:(b + 1) * HALF], ALU.mult, ALU.add)
                last.then_inc(x1_done, 1)
                dve.wait_ge(x1_done, i + 1)
                ln_stats(NT + i)
                ln_apply(NT + i)
                for _ in range(QUANT_AT[i]):
                    quantise(m)
                    m += 1
            dve.sem_inc(up_free, 4)
            dve.sem_inc(relu_free, 4)
            dve.sem_inc(out_done, 2)

            def hid_low(before, f, u, number):
                dve.wait_ge(hid_hi, before + 1)
                nc.vector.tensor_tensor(hid[:, bass.ds(f, 1), 1, 0:number], relu_tile(u, number),
                                        hid[:, bass.ds(f, 1), 0, 0:number], ALU.subtract).then_inc(relu_free, 1)

            for b, (first, number) in enumerate(BLOCKS):
                if b == 0:
                    for f in range(KF):
                        quantise(NCH + f)
                        hid_low(f, f, f % 4, number)
                else:
                    with dve.Fori(0, KF // 4) as q:
                        for u in range(4):
                            hid_low(q * 4 + (b * KF + u), q * 4 + u, u, number)
                for i in range(first // TILE, (first + number) // TILE):
                    dve.wait_ge(down_done, i + 1)
                    dve.wait_ge(res_in[i % 2], 16 * (i // 2 + 1))
                    if i < 2:
                        dve.wait_ge(x1b_stored[i], 16 * NT // 2)
                    else:
                        dve.wait_ge(stored[i % 2], 16 * (i // 2))
                    for c in range(2):
                        last = nc.vector.scalar_tensor_tensor(
                            ev[0:TILE, i % 2, c * HALF:(c + 1) * HALF], ps[0:TILE, DOWN_BANKS[i % 2] + c, :],
                            i_hid[0:TILE, :], xt[0:TILE, i % 2, c * HALF:(c + 1) * HALF], ALU.mult, ALU.add)
                    last.then_inc(out_done, 1)

        @block.tensor
        def _(pe):
            for v in range(2):
                pe.sem_inc(hot_free[v], 1)
            pe.wait_ge(consts_done, 1)
            for c in range(ET):
                chunk = c // DEG_TILES
                if c % DEG_TILES == 0:
                    pe.wait_ge(hot_done, chunk + 1)
                last = nc.tensor.matmul(ps[0:TILE, SUM_BANK, 0:NT], hot_lo[0:TILE, chunk % DEG_RING, :, c % DEG_TILES],
                                        hot_hi[0:TILE, c, :], start=(c == 0), stop=(c == ET - 1))
                if c % DEG_TILES == DEG_TILES - 1:
                    last.then_inc(hot_used, 1)
            pe.wait_ge(squares_in, 1)
            nc.tensor.matmul(ps[:, H_BANK + 1, 0:2], ones[:, :], part[:, 0:2], start=True,
                             stop=True).then_inc(squares_sum, 1)

            def turn(k):
                pe.wait_ge(xn_done, k + 1)
                if k >= 1:
                    pe.wait_ge(turned_hi, k)
                for b in range(KD):
                    last = nc.tensor.transpose(ps[:, TURN_BANK + b // 4, (b % 4) * TILE:(b % 4 + 1) * TILE],
                                               xn[0:TILE, k % 2, b * P:(b + 1) * P], ident[0:TILE, 0:TILE])
                last.then_inc(turned, 1)

            turn(0)
            pe.wait_ge(degrees_done, 1)
            pe.wait_ge(table_done, 1)
            largest = load_peak(pe)
            for t in range(NT):
                _, number, before = load_table(pe, t)
                if t >= 1:
                    pe.wait_ge(c_hi, t)
                    pe.wait_ge(c_out, t)
                pe.wait_ge(hot[0], before + t + 1)
                for b, (a, w) in enumerate(SRC_COLS):
                    last = nc.tensor.matmul(ps[0:TILE, C_BANK + b, 0:w], ident16[0:TILE, 0:TILE],
                                            one_src[0:TILE, 0, a:a + w], start=True, stop=False,
                                            skip_group_check=True)
                last.then_inc(hot_free[0], 1)
                with pe.Fori(0, number) as step:
                    for v in range(2):
                        pe.wait_ge(hot[v], before + step + (1 if v else t + 2))
                        for g in range(v * GROUP, (v + 1) * GROUP):
                            for b, (a, w) in enumerate(SRC_COLS):
                                last = nc.tensor.matmul(ps[0:TILE, C_BANK + b, 0:w], one_dst[0:TILE, g, :],
                                                        one_src[0:TILE, g, a:a + w],
                                                        start=False, stop=False, skip_group_check=True)
                        last.then_inc(hot_free[v], 1)
                pe.drain().then_inc(c_done, 1)
                if t + 1 < NT:
                    turn(t + 1)
                pe.wait_ge(ln_done, t + 1)
                if t >= 1:
                    pe.wait_ge(h_out, t)
                for k in range(KD):
                    if t == 0:
                        pe.wait_ge(wg_done, k + 1)
                    for s, v in ((0, 0), (0, 1), (1, 0)):
                        for c in range(2):
                            last = nc.tensor.matmul(ps[0:TILE, H_BANK + c, :], ln_t[:, s, k, t * TILE:(t + 1) * TILE],
                                                    wg[:, v, k, c * HALF:(c + 1) * HALF],
                                                    start=(k == 0 and s == 0 and v == 0), stop=(k == KD - 1 and s == 1))
                last.then_inc(h_done, 1)

            def aggregate(i, counts, j, start, stop):
                for s in range(2):
                    for c in range(2):
                        last = nc.tensor.matmul(ps[0:TILE, AGG_BANKS[i % 2] + c, :],
                                                counts[0:TILE, j, i * TILE:(i + 1) * TILE],
                                                h[0:TILE, s, j, c * HALF:(c + 1) * HALF],
                                                start=(start and s == 0), stop=(stop and s == 1),
                                                skip_group_check=True)
                return last

            pe.wait_ge(c_hi, NT)
            pe.wait_ge(c_out, NT)
            for i in range(NT):
                if i < 2:
                    pe.wait_ge(h_out, NT)
                else:
                    pe.wait_ge(x1_done, i - 1)
                for j in range(NT):
                    if i == 0:
                        pe.wait_ge(h_ready, j + 1)
                    last = aggregate(i, ct, j, j == 0, j == NT - 1)
                    if i == 0 and j == 2:
                        pe.wait_ge(w_sum_in, 1)
                        nc.tensor.matmul(ps[:, SUM_BANK, 0:2], ones[:, :], part[:, 0:2], start=True,
                                         stop=True).then_inc(w_sum, 1)
                    if j == NT - 2:
                        if i == 0:
                            pe.wait_ge(h_ready, NT)
                        with pe.If(largest > EXACT16):
                            for jj in range(NT):
                                aggregate(i, ct_lo, jj, False, False)
                last.then_inc(agg_done, 1)
                if i >= 1:
                    turn(NT + i - 1)

            pe.wait_ge(w_quant, NCH)
            for b, (first, number) in enumerate(BLOCKS):
                if b == 0:
                    pe.wait_ge(ln_done, NT + number // TILE)
                if b == 1:
                    pe.wait_ge(ln_done, 2 * NT)
                for f in range(KF):
                    pe.wait_ge(up_free, b * KF + f + 1)
                    if b == 0 and f == 2:
                        turn(2 * NT - 1)
                    for k in range(KD):
                        for s in range(2):
                            last = nc.tensor.matmul(ps[:, UP_BANKS[f % 4], 0:number], w1q[:, k, f * P:(f + 1) * P],
                                                    ln_t[:, s, k, first:first + number],
                                                    start=(k == 0 and s == 0), stop=(k == KD - 1 and s == 1))
                    last.then_inc(up_done, 1)
                if b == 0:
                    pe.wait_ge(w_quant, 2 * NCH - 4)
                tiles = range(first // TILE, (first + number) // TILE)
                for i in tiles:
                    if i == tiles[0]:
                        pe.wait_ge(relu_free, KF * (b + 1))
                    pe.wait_ge(out_done, i + 1)
                    for f in range(KF):
                        if i == tiles[0] and f == KF - 4:
                            pe.wait_ge(relu_free, 4 + KF * (b + 1))
                            if b == 0:
                                pe.wait_ge(w_quant, 2 * NCH)
                        for s in range(2):
                            for c in range(2):
                                last = nc.tensor.matmul(ps[0:TILE, DOWN_BANKS[i % 2] + c, :],
                                                        hid[:, f, s, i * TILE - first:(i + 1) * TILE - first],
                                                        w2q[:, f, c * HALF:(c + 1) * HALF],
                                                        start=(f == 0 and s == 0),
                                                        stop=(f == KF - 1 and s == 1))
                    last.then_inc(down_done, 1)


_INS = ["x", "src_t", "dst_t", "dst_g", "wg_t", "bg", "w1_t", "b1", "w2_t", "b2"]


def kernel(x, src, dst, L0_gnn_W, L0_gnn_b, L0_ffn_W1, L0_ffn_b1, L0_ffn_W2, L0_ffn_b2):
    import numpy as np
    import concourse.bacc as bacc
    from concourse.bass_utils import run_bass_kernel_spmd

    lay = np.ascontiguousarray
    arrays = {
        "x": lay(x),
        "src_t": lay(np.asarray(src).reshape(ET, TILE).T),
        "dst_t": lay(np.asarray(dst).reshape(ET, TILE).T),
        "dst_g": lay(np.asarray(dst).reshape(EG, GROUP * TILE)),
        "wg_t": lay(np.asarray(L0_gnn_W).T),
        "bg": lay(L0_gnn_b),
        "w1_t": lay(np.asarray(L0_ffn_W1).T),
        "b1": lay(np.asarray(L0_ffn_b1).reshape(KF, P).T),
        "w2_t": lay(np.asarray(L0_ffn_W2).T),
        "b2": lay(L0_ffn_b2),
    }
    nc = bacc.Bacc("TRN2", target_bir_lowering=False, num_devices=1)
    args = [nc.dram_tensor(n, arrays[n].shape, mybir.dt.from_np(arrays[n].dtype), kind="ExternalInput").ap()
            for n in _INS]
    out = nc.dram_tensor("out", (NODES, D), F32, kind="ExternalOutput").ap()
    gnn_ffn(nc, *args, out)
    r = run_bass_kernel_spmd(nc, [arrays], core_ids=[0])
    return r.results[0]["out"]
```
